# Optimizing a Trainium2 kernel written in Bass

```python
import numpy as np
import jax
import jax.numpy as jnp

def _softmax(x, axis=-1):
    return jax.nn.softmax(x, axis=axis)

def _gelu(x):
    return jax.nn.gelu(x, approximate=True)

def _silu(x):
    return jax.nn.silu(x)

def _sigmoid(x):
    return jax.nn.sigmoid(x)

def _layernorm(x, axis=-1, eps=1e-05):
    m = jnp.mean(x, axis=axis, keepdims=True)
    v = jnp.var(x, axis=axis, keepdims=True)
    return (x - m) / jnp.sqrt(v + eps)

def _scatter_add(tgt, idx, src, axis=0):
    return tgt.at[idx].add(src)

def _segment_sum(src, seg, n):
    return jax.ops.segment_sum(src, seg, n)
kernel_name = 'mk_xattn_seq_d1_seqx_r4_5ea32c'

def setup_inputs(seed: int=0):
    np.random.seed(seed)
    _w = jnp.asarray

    def _rec_inputs():
        import jax
        import jax.numpy as jnp
        _rk = jax.random.key(seed)
        x = -0.000125 + 0.9999 * jax.random.normal(jax.random.fold_in(_rk, 1), (32, 128, 1024), jnp.float32)
        _lenS = 128 - jax.random.randint(jax.random.fold_in(_rk, 7), (32,), 0, max(1, 128 // 4) + 1, jnp.int32)
        _lenS2 = 128 - jax.random.randint(jax.random.fold_in(_rk, 8), (32,), 0, max(1, 128 // 4) + 1, jnp.int32)
        _ctx_4096P = jax.random.normal(jax.random.fold_in(_rk, 11), (32, 16, 1024), jnp.float32)
        _ctx_4096c = jax.random.dirichlet(jax.random.fold_in(_rk, 511), 0.3 * jnp.ones((16,), jnp.float32), (32, 128))
        _ctx_4096t = jnp.einsum('bsk,bkd->bsd', _ctx_4096c, _ctx_4096P)
        _ctx_4096t = _ctx_4096t * jax.lax.rsqrt(jnp.mean(jnp.square(_ctx_4096t)) + 1e-12) * 0.953939
        ctx_4096 = -1.52775e-05 + 0.999936 * (_ctx_4096t + 0.3 * jax.random.normal(jax.random.fold_in(_rk, 611), (32, 128, 1024), jnp.float32))
        return (x, ctx_4096)
    x, ctx_4096 = _rec_inputs()

    def _L0_xattn_setup():
        import jax, jax.numpy as jnp
        import numpy as np
        NUM_HEADS = 8
        EPS = 1e-05

        def _conv1x1(W, b, t):
            return jnp.einsum('oc,bcl->bol', W, t) + b[None, :, None]
        key = jax.random.key(seed)
        ks = jax.random.split(key, 12)
        B, C, E, L = (16, 128, 128, 1024)
        s = lambda k, shape, sc=1.0: jax.random.normal(k, shape, dtype=jnp.float32) * sc
        return {'x': s(ks[0], (B, E, L)), 'y': s(ks[1], (B, C, L)), 'Wq': s(ks[2], (E, C), 0.02), 'bq': jnp.zeros((E,), jnp.float32), 'Wk': s(ks[3], (E, C), 0.02), 'bk': jnp.zeros((E,), jnp.float32), 'Wv': s(ks[4], (E, E), 0.02), 'bv': jnp.zeros((E,), jnp.float32), 'Wo': s(ks[5], (E, E), 0.02), 'bo': jnp.zeros((E,), jnp.float32), 'gn_w': jnp.ones((E,), jnp.float32), 'gn_b': jnp.zeros((E,), jnp.float32)}
    _L0_xattn_all = _L0_xattn_setup()
    _L0_xattn_in = {k: v for k, v in _L0_xattn_all.items() if k in ('Wq', 'bq', 'Wk', 'bk', 'Wv', 'bv', 'Wo', 'bo', 'gn_w', 'gn_b')}
    del _L0_xattn_all
    return {'x': x, 'ctx_4096': ctx_4096, 'L0_xattn_Wq': _L0_xattn_in['Wq'], 'L0_xattn_bq': _L0_xattn_in['bq'], 'L0_xattn_Wk': _L0_xattn_in['Wk'], 'L0_xattn_bk': _L0_xattn_in['bk'], 'L0_xattn_Wv': _L0_xattn_in['Wv'], 'L0_xattn_bv': _L0_xattn_in['bv'], 'L0_xattn_Wo': _L0_xattn_in['Wo'], 'L0_xattn_bo': _L0_xattn_in['bo'], 'L0_xattn_gn_w': _L0_xattn_in['gn_w'], 'L0_xattn_gn_b': _L0_xattn_in['gn_b']}

def reference(x, ctx_4096, L0_xattn_Wq, L0_xattn_bq, L0_xattn_Wk, L0_xattn_bk, L0_xattn_Wv, L0_xattn_bv, L0_xattn_Wo, L0_xattn_bo, L0_xattn_gn_w, L0_xattn_gn_b):
    import jax
    import jax.numpy as jnp

    def _L0_xattn_ref(x, y, Wq, bq, Wk, bk, Wv, bv, Wo, bo, gn_w, gn_b):
        import jax, jax.numpy as jnp
        import numpy as np
        NUM_HEADS = 8
        EPS = 1e-05

        def _conv1x1(W, b, t):
            return jnp.einsum('oc,bcl->bol', W, t) + b[None, :, None]
        B, E, Lx = x.shape
        H = NUM_HEADS
        Dh = E // H
        q = _conv1x1(Wq, bq, y).reshape(B, H, Dh, -1)
        k = _conv1x1(Wk, bk, y).reshape(B, H, Dh, -1)
        v = _conv1x1(Wv, bv, x).reshape(B, H, Dh, Lx)
        scores = jnp.einsum('bhdl,bhel->bhde', q, k) / jnp.sqrt(jnp.float32(E))
        attn = jax.nn.softmax(scores, axis=-1)
        out = jnp.einsum('bhde,bhel->bhdl', attn, v).reshape(B, E, Lx)
        o = _conv1x1(Wo, bo, out) + x
        mu = jnp.mean(o, axis=(1, 2), keepdims=True)
        var = jnp.var(o, axis=(1, 2), keepdims=True)
        o_hat = (o - mu) * jax.lax.rsqrt(var + EPS)
        return o_hat * gn_w[None, :, None] + gn_b[None, :, None]
    x = _L0_xattn_ref(x, ctx_4096, L0_xattn_Wq, L0_xattn_bq, L0_xattn_Wk, L0_xattn_bk, L0_xattn_Wv, L0_xattn_bv, L0_xattn_Wo, L0_xattn_bo, L0_xattn_gn_w, L0_xattn_gn_b)
    return x

_drawn_inputs = setup_inputs


def setup_inputs(seed=0):
    import zlib

    import numpy as np

    out = dict(_drawn_inputs(seed))
    spreads = {'L0_xattn_bq': (0.0, 0.575),
     'L0_xattn_bk': (0.0, 0.575),
     'L0_xattn_bv': (0.0, 0.678),
     'L0_xattn_bo': (0.0, 0.1),
     'L0_xattn_gn_w': (1.0, 0.2),
     'L0_xattn_gn_b': (0.0, 0.1)}
    factors = {'ctx_4096': 4.089, 'L0_xattn_Wq': 2.903, 'L0_xattn_Wk': 2.724}
    for name, (base, spread) in spreads.items():
        noise = np.random.default_rng([zlib.crc32(name.encode()), seed]).standard_normal(out[name].shape)
        drawn = base * np.exp(spread * noise) if base else spread * noise
        out[name] = jnp.asarray(drawn.astype(out[name].dtype))
    for name, factor in factors.items():
        out[name] = (out[name] * factor).astype(out[name].dtype)
    return out
```

```python
from contextlib import ExitStack

import concourse.bass as bass
from concourse import mybir

ALU = mybir.AluOpType
ACT = mybir.ActivationFunctionType
F32 = mybir.dt.float32
F32R = mybir.dt.float32r

HEADS = 8
EPS = 1e-5
OFF_HEAD = 1e30
UNROLL = 4
LAGS = 4
N_VECS = 7


def xattn_groupnorm_kernel(nc, x, yT, WqT, bq, WkT, bk, Wv, bv, WoT, bo, gn_w, gn_b, out):
    B, E, L = x.shape
    C = yT.shape[2]
    P = 128
    assert E == P and C == P and L % (4 * P) == 0 and B % UNROLL == 0
    DH = E // HEADS
    CH = L // P
    HALF = L // 2
    HCH = CH // 2
    SCALE = float(E) ** -0.5

    with ExitStack() as ctx:
        def sb(name, shape, dt=F32):
            return ctx.enter_context(nc.sbuf_tensor(name, shape, dt))

        def ps(name, shape, dt=F32):
            return ctx.enter_context(nc.psum_tensor(name, shape, dt))

        def sem(name):
            return ctx.enter_context(nc.semaphore(name))

        y_sb = sb("y_sb", [P, UNROLL, CH, C])
        x_sb = sb("x_sb", [P, UNROLL, L])
        out_sb = sb("out_sb", [P, UNROLL, L])
        hl_sb = sb("hl_sb", [P, 2, CH, 2, C], F32R)
        ysum4 = sb("ysum4", [P, CH // 2, C])
        ysum2 = sb("ysum2", [P, CH // 4, C])
        ysum = sb("ysum", [P, C])
        b2_sb = sb("b2_sb", [P, C], F32R)
        g_sb = sb("g_sb", [P, C])
        s_sb = sb("s_sb", [P, 1])
        p_sb = sb("p_sb", [P, E])
        sbk_sb = sb("sbk_sb", [P, E])
        sc_sb = sb("sc_sb", [P, E])
        a_sb = sb("a_sb", [P, E])
        r_sb = sb("r_sb", [P, E])
        m_sb = sb("m_sb", [P, E + 1])
        smin = sb("smin", [P, 2])
        zsum = sb("zsum", [P, 2])
        zinv = sb("zinv", [P, 2])
        bn = sb("bn", [P, 2, 2, 6])
        mv = sb("mv", [P, 2, 2])
        mrow = sb("mrow", [P, 2])
        dev = sb("dev", [P, 2])
        vrow = sb("vrow", [P, 2])
        veps = sb("veps", [P, 2])
        rstd = sb("rstd", [P, 2])
        nshift = sb("nshift", [P, 2])
        gain = sb("gain", [P, 2])
        shift = sb("shift", [P, 2])
        w_in = sb("w_in", [P, 4, P])
        wkT, woT, wv = w_in[:, 1, :], w_in[:, 2, :], w_in[:, 3, :]
        wqT = sb("wqT", [P, P])
        ident = sb("ident", [P, P + 1])
        ident_r = sb("ident_r", [P, P], F32R)
        onesn = sb("onesn", [P, P])
        ones = sb("ones", [P, 1])
        mask = sb("mask", [P, HEADS, DH])
        bq_raw = sb("bq_raw", [P, E])
        bqB = sb("bqB", [P, E])
        bkB = sb("bkB", [P, E])
        bq_col = sb("bq_col", [P, 1])
        k0 = sb("k0", [P, E])
        cols = sb("cols", [P, 4])
        nhalf = sb("nhalf", [P, 1])

        g_ps = ps("g_ps", [P, 512])
        sm_ps = ps("sm_ps", [P, 4, P])
        m_ps = ps("m_ps", [P, 512])
        st_ps = ps("st_ps", [P, 512])
        o_ps = ps("o_ps", [P, 2, L])
        mu_ps, var_ps, s_ps = st_ps[:, 0:1], st_ps[:, 8:9], st_ps[:, 16:17]

        y_in = [sem(f"y_in{k}") for k in range(UNROLL)]
        x_in = [sem(f"x_in{k}") for k in range(UNROLL)]
        out_done = [sem(f"out_done{k}") for k in range(UNROLL)]
        w_loaded = sem("w_loaded")
        c_loaded = sem("c_loaded")
        const_pool = sem("const_pool")
        const_dve = sem("const_dve")
        h_ready = sem("h_ready")
        l_ready = sem("l_ready")
        ysum4_ready = sem("ysum4_ready")
        ysum2_ready = sem("ysum2_ready")
        ysum_ready = sem("ysum_ready")
        hl_ready = sem("hl_ready")
        b2_copied = sem("b2_copied")
        g_ready = sem("g_ready")
        g_copied = sem("g_copied")
        s_ready = sem("s_ready")
        s_copied = sem("s_copied")
        p_ready = sem("p_ready")
        p_copied = sem("p_copied")
        sbk_ready = sem("sbk_ready")
        sc_ready = sem("sc_ready")
        smin_ready = sem("smin_ready")
        exp_done = sem("exp_done")
        zinv_ready = sem("zinv_ready")
        a_ready = sem("a_ready")
        r_ready = sem("r_ready")
        r_copied = sem("r_copied")
        m_ready = sem("m_ready")
        m_copied = sem("m_copied")
        o_ready = sem("o_ready")
        bn_done = sem("bn_done")
        mv_ready = sem("mv_ready")
        mrow_ready = sem("mrow_ready")
        mu_ready = sem("mu_ready")
        dev_ready = sem("dev_ready")
        vrow_ready = sem("vrow_ready")
        var_ready = sem("var_ready")
        veps_ready = sem("veps_ready")
        rstd_ready = sem("rstd_ready")
        nshift_ready = sem("nshift_ready")
        gain_ready = sem("gain_ready")
        affine_ready = sem("affine_ready")
        normed = sem("normed")

        def has(t, lag):
            return not isinstance(t, int) or 0 <= t - lag < B

        def exists(t, lag):
            return not isinstance(t, int) or t - lag >= 0

        def slot_count(t0, k, lag):
            return t0 * (16 // UNROLL) + 16 * ((k - lag) // UNROLL + 1)

        def pipeline(eng, step, first=UNROLL, end=B):
            for t in range(first):
                step(t - t % UNROLL, t % UNROLL)
            with eng.Fori(first, end - UNROLL + 1, UNROLL) as t0:
                for k in range(UNROLL):
                    step(t0, k)
            for t in range(end, B + LAGS):
                step(t - t % UNROLL, t % UNROLL)

        def batch(dram, b):
            return dram[bass.ds(b, 1)].rearrange("a p l -> p (a l)")

        def batch_y(b):
            return yT[bass.ds(b, 1)].rearrange("a (p j) c -> p (a j c)", p=P)

        def y_slot(k):
            return y_sb[:, k, :, :].rearrange("p j c -> p (j c)")

        block = ctx.enter_context(nc.Block())

        @block.sync
        def _(sp):
            for k in range(UNROLL):
                sp.dma_start(y_slot(k), batch_y(k)).then_inc(y_in[k], 16)
                if k == 0:
                    for i, w in enumerate((WqT, WkT, WoT, Wv)):
                        sp.dma_start(w_in[:, i, :], w).then_inc(w_loaded, 16)
                    for dst, v in ((bq_raw, bq), (bkB, bk)):
                        sp.dma_start(dst[:, :], v.rearrange("(a e) -> a e", a=1).broadcast_to([P, E])).then_inc(c_loaded, 16)
                    for dst, v in ((cols[:, 0:1], bv), (cols[:, 1:2], gn_w), (cols[:, 2:3], gn_b), (cols[:, 3:4], bq),
                                   (ident[:, P:P + 1], bo)):
                        sp.dma_start(dst, v.rearrange("(e a) -> e a", a=1)).then_inc(c_loaded, 16)
            for k in range(UNROLL):
                sp.dma_start(x_sb[:, k, :], batch(x, k)).then_inc(x_in[k], 16)

            def step(t0, k):
                t = t0 + k
                if has(t + UNROLL, 0):
                    sp.wait_ge(l_ready, (t + 1) * 2)
                    sp.wait_ge(ysum4_ready, t + 1)
                    sp.dma_start(y_slot(k), batch_y(t + UNROLL)).then_inc(y_in[k], 16)
                if has(t + 1, 0) and exists(t, UNROLL - 1):
                    kx = (k + 1) % UNROLL
                    sp.wait_ge(o_ready, (t - (UNROLL - 2)) * 2)
                    sp.dma_start(x_sb[:, kx, :], batch(x, t + 1)).then_inc(x_in[kx], 16)
                if has(t, 4):
                    sp.wait_ge(normed, t - 3)
                    sp.dma_start(batch(out, t - 4), out_sb[:, k, :]).then_inc(out_done[k], 16)

            pipeline(sp, step, end=B - UNROLL)
            for k in range(UNROLL):
                sp.wait_ge(out_done[k], 16 * (B // UNROLL))

        @block.gpsimd
        def _(pool):
            nc.gpsimd.memset(ident[:, 0:P], 0.0).then_inc(const_pool, 1)
            nc.gpsimd.memset(mask[:, :, :], 0.0).then_inc(const_pool, 1)
            nc.gpsimd.memset(nhalf[:, :], -0.5).then_inc(const_pool, 1)
            pool.wait_ge(const_pool, 3)
            nc.gpsimd.affine_select(out=ident[:, 0:P], in_=ident[:, 0:P], compare_op=ALU.not_equal, fill=1.0,
                                    base=0, pattern=[[-1, P]], channel_multiplier=1).then_inc(const_pool, 1)
            nc.gpsimd.affine_select(out=mask[:, :, :], in_=mask[:, :, :], compare_op=ALU.is_ge, fill=OFF_HEAD,
                                    base=0, pattern=[[-DH, HEADS], [0, DH]], channel_multiplier=1).then_inc(const_pool, 1)
            pool.wait_ge(const_pool, 5)
            nc.gpsimd.affine_select(out=mask[:, :, :], in_=mask[:, :, :], compare_op=ALU.is_ge, fill=OFF_HEAD,
                                    base=DH - 1, pattern=[[DH, HEADS], [0, DH]], channel_multiplier=-1).then_inc(const_pool, 1)

            def step(t0, k):
                t = t0 + k
                h = k % 2
                if has(t, 4):
                    pool.wait_ge(dev_ready, t - 3)
                    nc.gpsimd.tensor_tensor(nshift[:, h:h + 1], dev[:, h:h + 1], mv[:, h, 0:1],
                                            ALU.subtract).then_inc(nshift_ready, 1)
                    pool.wait_ge(veps_ready, t - 3)
                    nc.gpsimd.tensor_tensor(rstd[:, h:h + 1], veps[:, h:h + 1], nhalf[:, :], ALU.pow).then_inc(rstd_ready, 1)
                    pool.wait_ge(rstd_ready, t - 3)
                    nc.gpsimd.tensor_tensor(gain[:, h:h + 1], rstd[:, h:h + 1], cols[:, 1:2], ALU.mult).then_inc(gain_ready, 1)
                    pool.wait_ge(c_loaded, 16 * N_VECS)
                    pool.wait_ge(nshift_ready, t - 3)
                    pool.wait_ge(gain_ready, t - 3)
                    nc.gpsimd.tensor_scalar(shift[:, h:h + 1], nshift[:, h:h + 1], gain[:, h:h + 1], cols[:, 2:3],
                                            ALU.mult, ALU.add).then_inc(affine_ready, 1)
                if has(t, 1):
                    pool.wait_ge(s_copied, t)
                    nc.gpsimd.tensor_tensor(sbk_sb[:, :], bkB[:, :], s_sb[:, :].broadcast_to([P, E]),
                                            ALU.mult).then_inc(sbk_ready, 1)
                if has(t, 0):
                    pool.wait_ge(y_in[k], slot_count(t0, k, 0))
                    if exists(t, 1):
                        pool.wait_ge(ysum2_ready, t)
                    nc.gpsimd.tensor_tensor(ysum4[:, :, :], y_sb[:, k, 0:HCH, :], y_sb[:, k, HCH:CH, :],
                                            ALU.add).then_inc(ysum4_ready, 1)
                    pool.wait_ge(ysum4_ready, t + 1)
                    if exists(t, 1):
                        pool.wait_ge(ysum_ready, t)
                    nc.gpsimd.tensor_tensor(ysum2[:, :, :], ysum4[:, 0:HCH // 2, :], ysum4[:, HCH // 2:HCH, :],
                                            ALU.add).then_inc(ysum2_ready, 1)
                    pool.wait_ge(ysum2_ready, t + 1)
                    if exists(t, 1):
                        pool.wait_ge(s_ready, t)
                    nc.gpsimd.tensor_tensor(ysum[:, :], ysum2[:, 0, :], ysum2[:, 1, :], ALU.add).then_inc(ysum_ready, 1)

            pool.wait_ge(c_loaded, 16 * N_VECS)
            pipeline(pool, step)

        @block.scalar
        def _(act):
            def step(t0, k):
                t = t0 + k
                h = k % 2
                if has(t, 2):
                    act.wait_ge(smin_ready, t - 1)
                    nc.scalar.activation(a_sb[:, :], sc_sb[:, :], ACT.Exp, bias=smin[:, h:h + 1], scale=-1.0,
                                         accum_out=zsum[:, h:h + 1]).then_inc(exp_done, 1)

                def round_half(half):
                    chunks = slice(half * HCH, (half + 1) * HCH)
                    nc.scalar.copy(hl_sb[:, h, chunks, 0, :], y_sb[:, k, chunks, :]).then_inc(h_ready, 1)

                if has(t, 0):
                    act.wait_ge(y_in[k], slot_count(t0, k, 0))
                    if exists(t, 2):
                        act.wait_ge(hl_ready, t - 1)
                    round_half(0)
                if has(t, 1):
                    act.wait_ge(hl_ready, t)
                    nc.scalar.copy(b2_sb[:, :], g_ps[:, C:2 * C]).then_inc(b2_copied, 1)
                if has(t, 0):
                    round_half(1)
                if has(t, 2):
                    act.wait_ge(r_ready, t - 1)
                    nc.scalar.copy(r_sb[:, :], sm_ps[:, 1, :]).then_inc(r_copied, 1)
                if has(t, 4):
                    act.wait_ge(affine_ready, t - 3)
                    if exists(t, 8):
                        act.wait_ge(out_done[k], slot_count(t0, k, 8))
                    nc.scalar.activation(out_sb[:, k, :], o_ps[:, h, :], ACT.Identity,
                                         bias=shift[:, h:h + 1], scale=gain[:, h:h + 1]).then_inc(normed, 1)

            pipeline(act, step, first=2 * UNROLL)

        @block.vector
        def _(dve):
            nc.vector.memset(onesn[:, :], 1.0 / E).then_inc(const_dve, 1)
            nc.vector.memset(ones[:, :], 1.0).then_inc(const_dve, 1)
            dve.wait_ge(const_pool, 6)
            nc.vector.tensor_copy(ident_r[:, :], ident[:, 0:P]).then_inc(const_dve, 1)
            dve.wait_ge(w_loaded, 16 * 4)
            nc.vector.tensor_scalar(wqT[:, :], w_in[:, 0, :], -SCALE, None, ALU.mult).then_inc(const_dve, 1)
            dve.wait_ge(c_loaded, 16 * N_VECS)
            nc.vector.tensor_scalar(bqB[:, :], bq_raw[:, :], -SCALE, None, ALU.mult).then_inc(const_dve, 1)
            nc.vector.tensor_scalar(bq_col[:, :], cols[:, 3:4], -SCALE * L, None, ALU.mult).then_inc(const_dve, 1)
            dve.wait_ge(const_dve, 6)
            nc.vector.scalar_tensor_tensor(out=k0[:, :], in0=bkB[:, :], scalar=bq_col[:, :],
                                           in1=mask[:, :, :].rearrange("p h d -> p (h d)"),
                                           op0=ALU.mult, op1=ALU.add).then_inc(const_dve, 1)

            def step(t0, k):
                t = t0 + k
                h = k % 2
                if has(t, 3):
                    if exists(t, 4):
                        dve.wait_ge(mrow_ready, t - 3)
                    dve.wait_ge(m_ready, t - 2)
                    nc.vector.tensor_tensor(m_sb[:, :], m_ps[:, 0:E + 1], ident[:, :], ALU.add).then_inc(m_copied, 1)
                if has(t, 2):
                    done = t - 1 if isinstance(t, int) else dve.to_reg(t - 1)
                    dve.wait_ge(const_dve, 7)
                    dve.wait_ge(sc_ready, done)
                    nc.vector.tensor_tensor_reduce(out=sc_sb[:, :], in0=sm_ps[:, 0, :], in1=k0[:, :], scale=1.0,
                                                   scalar=3e38, op0=ALU.add, op1=ALU.min,
                                                   accum_out=smin[:, h:h + 1]).then_inc(smin_ready, 1)
                if has(t, 4):
                    dve.wait_ge(mu_ready, t - 3)
                    nc.vector.tensor_tensor(dev[:, h:h + 1], mrow[:, h:h + 1], mu_ps, ALU.subtract).then_inc(dev_ready, 1)
                    dve.wait_ge(dev_ready, t - 3)
                    nc.vector.scalar_tensor_tensor(out=vrow[:, h:h + 1], in0=dev[:, h:h + 1], scalar=dev[:, h:h + 1],
                                                   in1=mv[:, h, 1:2], op0=ALU.mult, op1=ALU.add).then_inc(vrow_ready, 1)
                if has(t, 2):
                    dve.wait_ge(exp_done, t - 1)
                    nc.vector.reciprocal(zinv[:, h:h + 1], zsum[:, h:h + 1]).then_inc(zinv_ready, 1)
                    dve.wait_ge(zinv_ready, t - 1)
                    nc.vector.tensor_scalar(a_sb[:, :], a_sb[:, :], zinv[:, h:h + 1], None, ALU.mult).then_inc(a_ready, 1)
                if has(t, 4):
                    dve.wait_ge(var_ready, t - 3)
                    nc.vector.tensor_scalar(veps[:, h:h + 1], var_ps, EPS, None, ALU.add).then_inc(veps_ready, 1)

                def rest_half(half):
                    chunks = slice(half * HCH, (half + 1) * HCH)
                    dve.wait_ge(h_ready, t * 2 + 1 + half)
                    nc.vector.tensor_tensor(hl_sb[:, h, chunks, 1, :], y_sb[:, k, chunks, :],
                                            hl_sb[:, h, chunks, 0, :].bitcast(F32), ALU.subtract).then_inc(l_ready, 1)

                if has(t, 0):
                    rest_half(0)
                if has(t, 3):
                    dve.wait_ge(o_ready, (t - 3) * 2 + 1)
                    nc.vector.bn_stats(bn[:, 1 - h, 0, :], o_ps[:, 1 - h, 0:HALF])
                if has(t, 1):
                    dve.wait_ge(g_ready, t)
                    nc.vector.tensor_tensor(g_sb[:, :], g_ps[:, 0:C], b2_sb[:, :].bitcast(F32), ALU.add).then_inc(g_copied, 1)
                    dve.wait_ge(s_ready, t)
                    nc.vector.tensor_copy(s_sb[:, :], s_ps).then_inc(s_copied, 1)
                if has(t, 0):
                    rest_half(1)
                if has(t, 1):
                    dve.wait_ge(s_copied, t)
                    dve.wait_ge(p_ready, t)
                    nc.vector.scalar_tensor_tensor(out=p_sb[:, :], in0=bqB[:, :], scalar=s_sb[:, :],
                                                   in1=sm_ps[:, 2, :], op0=ALU.mult, op1=ALU.add).then_inc(p_copied, 1)
                if has(t, 3):
                    dve.wait_ge(o_ready, (t - 3) * 2 + 2)
                    nc.vector.bn_stats(bn[:, 1 - h, 1, :], o_ps[:, 1 - h, HALF:L]).then_inc(bn_done, 1)
                    dve.wait_ge(c_loaded, 16 * N_VECS)
                    dve.wait_ge(bn_done, t - 2)
                    nc.vector.bn_aggr(mv[:, 1 - h, :], bn[:, 1 - h, :, :].rearrange("p a b -> p (a b)")).then_inc(mv_ready, 1)
                    dve.wait_ge(mv_ready, t - 2)
                    nc.vector.tensor_tensor(mrow[:, 1 - h:2 - h], m_sb[:, E:E + 1], mv[:, 1 - h, 0:1],
                                            ALU.add).then_inc(mrow_ready, 1)

            pipeline(dve, step)

        @block.tensor
        def _(pe):
            pe.wait_ge(w_loaded, 16 * 4)
            pe.wait_ge(const_dve, 7)

            def product(dst, lhsT, rhs, start=True, stop=True, **more):
                return nc.tensor.matmul(dst, lhsT, rhs, start=start, stop=stop, **more)

            def step(t0, k):
                t = t0 + k
                h = k % 2
                if has(t, 2):
                    pe.wait_ge(p_copied, t - 1)
                    pe.wait_ge(sbk_ready, t - 1)
                    product(sm_ps[:, 0, :], p_sb[:, :], wkT, stop=False)
                    product(sm_ps[:, 0, :], wqT[:, :], sbk_sb[:, :], start=False).then_inc(sc_ready, 1)
                if has(t, 4):
                    pe.wait_ge(mrow_ready, t - 3)
                    product(mu_ps, onesn[:, :], mrow[:, h:h + 1]).then_inc(mu_ready, 1)
                if has(t, 1):
                    pe.wait_ge(l_ready, t * 2)
                    for c in range(CH):
                        mm = product(g_ps[:, 0:2 * C], hl_sb[:, 1 - h, c, 0, :],
                                     hl_sb[:, 1 - h, c, :, :].rearrange("p a c -> p (a c)"),
                                     start=(c == 0), stop=(c == CH - 1))
                    mm.then_inc(hl_ready, 1)
                if has(t, 4):
                    pe.wait_ge(vrow_ready, t - 3)
                    product(var_ps, onesn[:, :], vrow[:, h:h + 1]).then_inc(var_ready, 1)

                def products_of_x(half):
                    cols_of = slice(half * HALF, (half + 1) * HALF)
                    product(o_ps[:, 1 - h, cols_of], m_sb[:, 0:E], x_sb[:, (k - 3) % UNROLL, cols_of]).then_inc(o_ready, 1)

                if has(t, 3):
                    pe.wait_ge(m_copied, t - 2)
                    pe.wait_ge(x_in[(k - 3) % UNROLL], slot_count(t0, k, 3))
                    if exists(t, 5):
                        pe.wait_ge(normed, t - 4)
                    products_of_x(0)
                if has(t, 1):
                    pe.wait_ge(b2_copied, t)
                    product(g_ps[:, 0:C], b2_sb[:, :], ident_r[:, :], start=False, skip_group_check=True).then_inc(g_ready, 1)
                if has(t, 2):
                    pe.wait_ge(a_ready, t - 1)
                    product(sm_ps[:, 1, :], a_sb[:, :], woT).then_inc(r_ready, 1)
                if has(t, 1):
                    pe.wait_ge(ysum_ready, t)
                    if exists(t, 4):
                        pe.wait_ge(veps_ready, t - 3)
                    elif exists(t, 2):
                        pe.wait_ge(s_copied, t - 1)
                    product(s_ps, ysum[:, :], ones[:, :]).then_inc(s_ready, 1)
                if has(t, 3):
                    products_of_x(1)
                if has(t, 1):
                    pe.wait_ge(g_copied, t)
                    if exists(t, 2):
                        pe.wait_ge(r_copied, t - 1)
                    product(sm_ps[:, 2, :], g_sb[:, :], wqT[:, :]).then_inc(p_ready, 1)
                if has(t, 2):
                    pe.wait_ge(r_copied, t - 1)
                    product(m_ps[:, 0:E], wv, r_sb[:, :])
                    product(m_ps[:, E:E + 1], r_sb[:, :], cols[:, 0:1]).then_inc(m_ready, 1)

            pipeline(pe, step, first=2 * UNROLL)


_INS = ['x', 'ctx_4096', 'L0_xattn_Wq', 'L0_xattn_bq', 'L0_xattn_Wk', 'L0_xattn_bk', 'L0_xattn_Wv', 'L0_xattn_bv',
        'L0_xattn_Wo', 'L0_xattn_bo', 'L0_xattn_gn_w', 'L0_xattn_gn_b']
_TURNED = ['ctx_4096', 'L0_xattn_Wq', 'L0_xattn_Wk', 'L0_xattn_Wo']
_OUTS = [((32, 128, 1024), 'float32')]


def kernel(**inputs):
    import numpy as _np
    import concourse.bacc as _bacc
    from concourse import mybir as _mybir
    from concourse.bass_utils import run_bass_kernel_spmd as _run

    nc = _bacc.Bacc("TRN2", target_bir_lowering=False, num_devices=1)
    arrays, args = {}, []
    for name in _INS:
        a = _np.asarray(inputs[name])
        if name in _TURNED:
            a = _np.swapaxes(a, -1, -2)
        a = _np.ascontiguousarray(a)
        arrays[f"in_{name}_dram"] = a
        args.append(nc.dram_tensor(f"in_{name}_dram", a.shape, _mybir.dt.from_np(a.dtype), kind="ExternalInput").ap())
    for i, (shape, dtype) in enumerate(_OUTS):
        dt = _mybir.dt.from_np(_np.dtype(dtype))
        args.append(nc.dram_tensor(f"out_{i}_dram", shape, dt, kind="ExternalOutput").ap())
    xattn_groupnorm_kernel(nc, *args)
    r = _run(nc, [arrays], core_ids=[0])
    got = tuple(r.results[0][f"out_{i}_dram"] for i in range(len(_OUTS)))
    return got[0]
```

```python
from contextlib import ExitStack

import concourse.bass as bass
from concourse import mybir

ALU = mybir.AluOpType
ACT = mybir.ActivationFunctionType
F32 = mybir.dt.float32
F32R = mybir.dt.float32r

HEADS = 8
EPS = 1e-5
OFF_HEAD = 1e30
UNROLL = 4
N_CONST = 2
LAGS = 5
WARM_UP = 12
FILL = [3, 2, 4, 3, 0, 0]


def xattn_groupnorm_kernel(nc, x, yT, weights, biases, columns, out):
    B, E, L = x.shape
    C = yT.shape[2]
    P = 128
    assert E == P and C == P and L % (4 * P) == 0 and B % UNROLL == 0
    DH = E // HEADS
    CH = L // P
    HALF = L // 2
    HCH = CH // 2
    HL = 2 * C + 2
    SCALE = float(E) ** -0.5

    with ExitStack() as ctx:
        def sb(name, shape, dt=F32):
            return ctx.enter_context(nc.sbuf_tensor(name, shape, dt))

        def ps(name, shape, dt=F32):
            return ctx.enter_context(nc.psum_tensor(name, shape, dt))

        def sem(name):
            return ctx.enter_context(nc.semaphore(name))

        y_sb = sb("y_sb", [P, UNROLL, CH, C])
        x_sb = sb("x_sb", [P, UNROLL, L])
        out_sb = sb("out_sb", [P, UNROLL, L])
        hl_sb = sb("hl_sb", [P, UNROLL, CH, HL], F32R)
        lsum4 = sb("lsum4", [P, CH // 2, C])
        lsum2 = sb("lsum2", [P, CH // 4, C])
        lsum = sb("lsum", [P, 2, C], F32R)
        b2_sb = sb("b2_sb", [P, C], F32R)
        g_sb = sb("g_sb", [P, C])
        s_sb = sb("s_sb", [P, 1])
        p_sb = sb("p_sb", [P, E])
        sbk_sb = sb("sbk_sb", [P, E])
        sc_sb = sb("sc_sb", [P, E])
        a_sb = sb("a_sb", [P, E])
        r_sb = sb("r_sb", [P, E])
        m_sb = sb("m_sb", [P, 2, E + 1])
        smin = sb("smin", [P, 2])
        zsum = sb("zsum", [P, 2])
        zinv = sb("zinv", [P, 2])
        bn = sb("bn", [P, 2, 2, 6])
        mv = sb("mv", [P, 2, 2])
        mrow = sb("mrow", [P, 2])
        dev = sb("dev", [P, 2])
        vrow = sb("vrow", [P, 2])
        veps = sb("veps", [P, 2])
        rstd = sb("rstd", [P, 2])
        nshift = sb("nshift", [P, 2])
        gain = sb("gain", [P, 2])
        shift = sb("shift", [P, 2])
        w_in = sb("w_in", [P, 4, P])
        wkT, woT, wv = w_in[:, 1, :], w_in[:, 2, :], w_in[:, 3, :]
        wqT = sb("wqT", [P, P])
        ident = sb("ident", [P, P + 1])
        ident_r = sb("ident_r", [P, P], F32R)
        onesn = sb("onesn", [P, P])
        ones_r = sb("ones_r", [P, 2], F32R)
        mask = sb("mask", [P, HEADS, DH])
        rows = sb("rows", [P, 2, E])
        bqB = sb("bqB", [P, E])
        bq_col = sb("bq_col", [P, 1])
        k0 = sb("k0", [P, E])
        cols = sb("cols", [P, 6])
        bkB = rows[:, 1, :]
        bq_raw, bv, bo, gn_w, gn_b = cols[:, 0:1], cols[:, 2:3], cols[:, 3:4], cols[:, 4:5], cols[:, 5:6]
        nhalf = sb("nhalf", [P, 1])
        warm = sb("warm", [P, 1])

        g_ps = ps("g_ps", [P, 512])
        ps_ps = ps("ps_ps", [P, 4, P])
        rm_ps = ps("rm_ps", [P, 512])
        st_ps = ps("st_ps", [P, 512])
        o_ps = ps("o_ps", [P, 2, L])
        p_ps, sc_ps, r_ps, m_ps = ps_ps[:, 0, :], ps_ps[:, 1, :], rm_ps[:, 0:P], rm_ps[:, 256:256 + E + 1]
        mu_ps, var_ps, s_ps = st_ps[:, 0:1], st_ps[:, 8:9], g_ps[:, 2 * C:2 * C + 1]

        y_in = [sem(f"y_in{k}") for k in range(UNROLL)]
        x_in = [sem(f"x_in{k}") for k in range(UNROLL)]
        out_done = [sem(f"out_done{k}") for k in range(UNROLL)]
        w_loaded = sem("w_loaded")
        c_loaded = sem("c_loaded")
        const_pool = sem("const_pool")
        const_dve = sem("const_dve")
        h_ready = sem("h_ready")
        l_ready = sem("l_ready")
        lsum4_ready = sem("lsum4_ready")
        lsum2_ready = sem("lsum2_ready")
        lsum_ready = sem("lsum_ready")
        hl_ready = sem("hl_ready")
        b2_copied = sem("b2_copied")
        g_ready = sem("g_ready")
        g_copied = sem("g_copied")
        s_copied = sem("s_copied")
        p_ready = sem("p_ready")
        p_copied = sem("p_copied")
        sbk_ready = sem("sbk_ready")
        sc_ready = sem("sc_ready")
        smin_ready = sem("smin_ready")
        exp_done = sem("exp_done")
        zinv_ready = sem("zinv_ready")
        a_ready = sem("a_ready")
        r_ready = sem("r_ready")
        r_copied = sem("r_copied")
        m_ready = sem("m_ready")
        m_copied = sem("m_copied")
        o_ready = sem("o_ready")
        bn_done = sem("bn_done")
        mv_ready = sem("mv_ready")
        mrow_ready = sem("mrow_ready")
        mu_ready = sem("mu_ready")
        dev_ready = sem("dev_ready")
        vrow_ready = sem("vrow_ready")
        var_ready = sem("var_ready")
        veps_ready = sem("veps_ready")
        rstd_ready = sem("rstd_ready")
        nshift_ready = sem("nshift_ready")
        gain_ready = sem("gain_ready")
        affine_ready = sem("affine_ready")
        normed = sem("normed")
        normed_dve = sem("normed_dve")

        def has(t, lag):
            return not isinstance(t, int) or 0 <= t - lag < B

        def exists(t, lag):
            return not isinstance(t, int) or t - lag >= 0

        def late(t):
            return isinstance(t, int) and t == B + 2

        def last(t):
            return isinstance(t, int) and t == B + LAGS - 1

        def first_steps(t, which):
            return isinstance(t, int) and t == which

        def slot_count(t0, k, lag):
            return t0 * (16 // UNROLL) + 16 * ((k - lag) // UNROLL + 1)

        def pipeline(eng, step, begin=0, first=2 * UNROLL, end=B):
            for t in range(begin, first):
                step(t - t % UNROLL, t % UNROLL)
            with eng.Fori(first, end - UNROLL + 1, UNROLL) as t0:
                for k in range(UNROLL):
                    step(t0, k)
            for t in range(end, B + LAGS):
                step(t - t % UNROLL, t % UNROLL)

        def batch(dram, b):
            return dram[bass.ds(b, 1)].rearrange("a p l -> p (a l)")

        def batch_y(b):
            return yT[bass.ds(b, 1)].rearrange("a (p j) c -> p (a j c)", p=P)

        def y_slot(k):
            return y_sb[:, k, :, :].rearrange("p j c -> p (j c)")

        block = ctx.enter_context(nc.Block())

        @block.sync
        def _(sp):
            for k in range(UNROLL):
                sp.dma_start(y_slot(k), batch_y(k)).then_inc(y_in[k], 16)
            for k in range(UNROLL):
                sp.dma_start(x_sb[:, k, :], batch(x, k)).then_inc(x_in[k], 16)

            def step(t0, k):
                t = t0 + k
                if has(t + UNROLL - 1, 0) and exists(t, 1):
                    ky = (k - 1) % UNROLL
                    sp.wait_ge(l_ready, t * 2)
                    sp.dma_start(y_slot(ky), batch_y(t + UNROLL - 1)).then_inc(y_in[ky], 16)
                if has(t, 0) and exists(t, 4):
                    sp.wait_ge(o_ready, (t - (UNROLL - 1)) * 2)
                    sp.dma_start(x_sb[:, k, :], batch(x, t)).then_inc(x_in[k], 16)
                if last(t):
                    ko = (k - 5) % UNROLL
                    for half, done in ((0, normed), (1, normed_dve)):
                        part = slice(half * HALF, (half + 1) * HALF)
                        sp.wait_ge(done, B if half == 0 else 1)
                        sp.dma_start(batch(out, B - 1)[:, part], out_sb[:, ko, part]).then_inc(out_done[ko], 16)
                elif has(t, 5):
                    ko = (k - 5) % UNROLL
                    sp.wait_ge(normed, t - 4)
                    sp.dma_start(batch(out, t - 5), out_sb[:, ko, :]).then_inc(out_done[ko], 16)

            pipeline(sp, step, end=B - UNROLL)
            for k in range(UNROLL):
                sp.wait_ge(out_done[k], 16 * (B // UNROLL + (k == (B - 1) % UNROLL)))

        @block.gpsimd
        def _(pool):
            nc.gpsimd.memset(nhalf[:, :], -0.5).then_inc(const_pool, 1)
            nc.gpsimd.memset(ident[:, 0:P], 0.0).then_inc(const_pool, 1)
            nc.gpsimd.memset(mask[:, :, :], 0.0).then_inc(const_pool, 1)
            pool.wait_ge(const_pool, 3)
            nc.gpsimd.affine_select(out=ident[:, 0:P], in_=ident[:, 0:P], compare_op=ALU.not_equal, fill=1.0,
                                    base=0, pattern=[[-1, P]], channel_multiplier=1).then_inc(const_pool, 1)
            nc.gpsimd.affine_select(out=mask[:, :, :], in_=mask[:, :, :], compare_op=ALU.is_ge, fill=OFF_HEAD,
                                    base=0, pattern=[[-DH, HEADS], [0, DH]], channel_multiplier=1).then_inc(const_pool, 1)
            pool.wait_ge(const_pool, 5)
            nc.gpsimd.affine_select(out=mask[:, :, :], in_=mask[:, :, :], compare_op=ALU.is_ge, fill=OFF_HEAD,
                                    base=DH - 1, pattern=[[DH, HEADS], [0, DH]], channel_multiplier=-1).then_inc(const_pool, 1)

            def step(t0, k):
                t = t0 + k
                h = k % 2
                h1 = 1 - h
                if isinstance(t, int) and t == 5:
                    pool.wait_ge(c_loaded, 16 * N_CONST)
                if has(t, 5):
                    pool.wait_ge(dev_ready, t - 4)
                    nc.gpsimd.tensor_tensor(nshift[:, h1:h1 + 1], dev[:, h1:h1 + 1], mv[:, h1, 0:1],
                                            ALU.subtract).then_inc(nshift_ready, 1)
                    pool.wait_ge(veps_ready, t - 4)
                    nc.gpsimd.tensor_tensor(rstd[:, h1:h1 + 1], veps[:, h1:h1 + 1], nhalf[:, :], ALU.pow).then_inc(rstd_ready, 1)
                    pool.wait_ge(rstd_ready, t - 4)
                    nc.gpsimd.tensor_tensor(gain[:, h1:h1 + 1], rstd[:, h1:h1 + 1], gn_w, ALU.mult).then_inc(gain_ready, 1)
                    pool.wait_ge(c_loaded, 16 * N_CONST)
                    pool.wait_ge(nshift_ready, t - 4)
                    pool.wait_ge(gain_ready, t - 4)
                    nc.gpsimd.tensor_scalar(shift[:, h1:h1 + 1], nshift[:, h1:h1 + 1], gain[:, h1:h1 + 1], gn_b,
                                            ALU.mult, ALU.add).then_inc(affine_ready, 1)
                if has(t, 1):
                    low = hl_sb[:, (k - 1) % UNROLL, :, C:2 * C].bitcast(F32)
                    pool.wait_ge(l_ready, t * 2)
                    if exists(t, 2):
                        pool.wait_ge(lsum2_ready, t - 1)
                    nc.gpsimd.tensor_tensor(lsum4[:, :, :], low[:, 0:HCH, :], low[:, HCH:CH, :],
                                            ALU.add).then_inc(lsum4_ready, 1)
                    pool.wait_ge(lsum4_ready, t)
                    if exists(t, 2):
                        pool.wait_ge(lsum_ready, t - 1)
                    nc.gpsimd.tensor_tensor(lsum2[:, :, :], lsum4[:, 0:HCH // 2, :], lsum4[:, HCH // 2:HCH, :],
                                            ALU.add).then_inc(lsum2_ready, 1)
                    pool.wait_ge(lsum2_ready, t)
                    if exists(t, 3):
                        pool.wait_ge(g_ready, t - 2)
                    nc.gpsimd.tensor_tensor(lsum[:, h1, :], lsum2[:, 0, :], lsum2[:, 1, :], ALU.add).then_inc(lsum_ready, 1)

            pipeline(pool, step)

        @block.scalar
        def _(act):
            act.wait_ge(const_pool, 1)
            nc.scalar.activation(warm[:, :], nhalf[:, :], ACT.Exp)
            act.dma_start(cols[:, :], columns).then_inc(c_loaded, 16)
            act.dma_start(w_in[:, :, :].rearrange("p w c -> p (w c)"), weights).then_inc(w_loaded, 16)
            act.dma_start(rows[:, :, :].rearrange("p v e -> p (v e)"),
                          biases.rearrange("(a v) e -> a (v e)", a=1).broadcast_to([P, 2 * E])).then_inc(c_loaded, 16)

            def step(t0, k):
                t = t0 + k
                h = k % 2
                h1 = 1 - h
                if has(t, 3):
                    act.wait_ge(smin_ready, t - 2)
                    nc.scalar.activation(a_sb[:, :], sc_sb[:, :], ACT.Exp, bias=smin[:, h1:h1 + 1], scale=-1.0,
                                         accum_out=zsum[:, h1:h1 + 1]).then_inc(exp_done, 1)

                def round_half(half):
                    chunks = slice(half * HCH, (half + 1) * HCH)
                    nc.scalar.copy(hl_sb[:, k, chunks, 0:C], y_sb[:, k, chunks, :]).then_inc(h_ready, 1)

                if has(t, 0):
                    act.wait_ge(y_in[k], slot_count(t0, k, 0))
                    if exists(t, 4):
                        act.wait_ge(g_ready, t - 3)
                    round_half(0)
                if has(t, 2):
                    if isinstance(t, int) and t == 2:
                        act.wait_ge(c_loaded, 16 * N_CONST)
                    act.wait_ge(s_copied, t - 1)
                    nc.scalar.mul(sbk_sb[:, :], bkB, s_sb[:, :]).then_inc(sbk_ready, 1)
                if has(t, 3):
                    act.wait_ge(r_ready, t - 2)
                    nc.scalar.copy(r_sb[:, :], r_ps).then_inc(r_copied, 1)
                if has(t, 5):
                    ko = (k - 5) % UNROLL
                    act.wait_ge(affine_ready, t - 4)
                    if exists(t, 9):
                        act.wait_ge(out_done[ko], slot_count(t0, k, 9))
                    part = slice(0, HALF if last(t) else L)
                    nc.scalar.activation(out_sb[:, ko, part], o_ps[:, h1, part], ACT.Identity,
                                         bias=shift[:, h1:h1 + 1], scale=gain[:, h1:h1 + 1]).then_inc(normed, 1)
                early = isinstance(t, int) and t < 2
                if has(t, 0) and early:
                    round_half(1)
                if has(t, 1):
                    act.wait_ge(hl_ready, t)
                    nc.scalar.copy(b2_sb[:, :], g_ps[:, C:2 * C]).then_inc(b2_copied, 1)
                if has(t, 0) and not early:
                    round_half(1)

            pipeline(act, step, first=3 * UNROLL)

        @block.vector
        def _(dve):
            nc.vector.memset(onesn[:, :], 1.0 / E).then_inc(const_dve, 1)
            nc.vector.memset(ones_r[:, :].bitcast(F32), 1.0).then_inc(const_dve, 1)
            nc.vector.memset(hl_sb[:, :, :, 2 * C:HL].bitcast(F32), 1.0).then_inc(const_dve, 1)
            dve.wait_ge(const_pool, 6)
            nc.vector.tensor_copy(ident_r[:, :], ident[:, 0:P]).then_inc(const_dve, 1)

            def value(v):
                return v if isinstance(v, int) else dve.to_reg(v)

            def step(t0, k):
                t = t0 + k
                h = k % 2
                h1 = 1 - h
                if has(t, 4):
                    dve.wait_ge(m_ready, t - 3)
                    nc.vector.tensor_tensor(m_sb[:, h, :], m_ps, ident[:, :], ALU.add).then_inc(m_copied, 1)
                if has(t, 5):
                    dve.wait_ge(mu_ready, t - 4)
                    nc.vector.tensor_tensor(dev[:, h1:h1 + 1], mrow[:, h1:h1 + 1], mu_ps, ALU.subtract).then_inc(dev_ready, 1)
                    dve.wait_ge(dev_ready, t - 4)
                    nc.vector.scalar_tensor_tensor(out=vrow[:, h1:h1 + 1], in0=dev[:, h1:h1 + 1], scalar=dev[:, h1:h1 + 1],
                                                   in1=mv[:, h1, 1:2], op0=ALU.mult, op1=ALU.add).then_inc(vrow_ready, 1)
                if has(t, 3):
                    done = value(t - 2)
                    dve.wait_ge(const_dve, 9)
                    dve.wait_ge(sc_ready, done)
                    nc.vector.tensor_tensor_reduce(out=sc_sb[:, :], in0=sc_ps, in1=k0[:, :], scale=1.0,
                                                   scalar=3e38, op0=ALU.add, op1=ALU.min,
                                                   accum_out=smin[:, h1:h1 + 1]).then_inc(smin_ready, 1)

                def rest_half(b, half):
                    ky = (k + b) % UNROLL
                    chunks = slice(half * HCH, (half + 1) * HCH)
                    dve.wait_ge(h_ready, (t + b) * 2 + 1 + half)
                    nc.vector.tensor_tensor(hl_sb[:, ky, chunks, C:2 * C], y_sb[:, ky, chunks, :],
                                            hl_sb[:, ky, chunks, 0:C].bitcast(F32), ALU.subtract).then_inc(l_ready, 1)

                if has(t, 1):
                    rest_half(-1, 1)
                def inverse_sums():
                    dve.wait_ge(exp_done, t - 2)
                    nc.vector.reciprocal(zinv[:, h1:h1 + 1], zsum[:, h1:h1 + 1]).then_inc(zinv_ready, 1)

                def variance():
                    dve.wait_ge(var_ready, t - 4)
                    nc.vector.tensor_scalar(veps[:, h1:h1 + 1], var_ps, EPS, None, ALU.add).then_inc(veps_ready, 1)

                def gram():
                    dve.wait_ge(g_ready, t - 1)
                    nc.vector.tensor_tensor(g_sb[:, :], g_ps[:, 0:C], b2_sb[:, :].bitcast(F32), ALU.add).then_inc(g_copied, 1)
                    nc.vector.tensor_copy(s_sb[:, :], s_ps).then_inc(s_copied, 1)

                def statistics():
                    dve.wait_ge(o_ready, (t - 4) * 2 + 1)
                    nc.vector.bn_stats(bn[:, h, 0, :], o_ps[:, h, 0:HALF])
                    dve.wait_ge(o_ready, (t - 3) * 2)
                    nc.vector.bn_stats(bn[:, h, 1, :], o_ps[:, h, HALF:L]).then_inc(bn_done, 1)

                def query_product():
                    dve.wait_ge(s_copied, t - 1)
                    dve.wait_ge(p_ready, t - 1)
                    nc.vector.scalar_tensor_tensor(out=p_sb[:, :], in0=bqB[:, :], scalar=s_sb[:, :],
                                                   in1=p_ps, op0=ALU.mult, op1=ALU.add).then_inc(p_copied, 1)

                if has(t, 5) and late(t):
                    variance()
                if has(t, 3):
                    inverse_sums()
                if has(t, 5) and not late(t):
                    variance()
                if has(t, 3):
                    dve.wait_ge(zinv_ready, t - 2)
                    nc.vector.tensor_scalar(a_sb[:, :], a_sb[:, :], zinv[:, h1:h1 + 1], None, ALU.mult).then_inc(a_ready, 1)
                if has(t, 2):
                    gram()
                if has(t, 4):
                    statistics()
                if has(t, 2):
                    query_product()
                if has(t, 4):
                    done = value(t - 3)
                    dve.wait_ge(c_loaded, 16 * N_CONST)
                    dve.wait_ge(bn_done, done)
                    nc.vector.bn_aggr(mv[:, h, :], bn[:, h, :, :].rearrange("p a b -> p (a b)")).then_inc(mv_ready, 1)
                    dve.wait_ge(mv_ready, t - 3)
                    nc.vector.tensor_tensor(mrow[:, h:h + 1], m_sb[:, h, E:E + 1], mv[:, h, 0:1],
                                            ALU.add).then_inc(mrow_ready, 1)
                if has(t, 0):
                    rest_half(0, 0)
                if last(t):
                    ko = (k - 5) % UNROLL
                    dve.wait_ge(affine_ready, B)
                    dve.wait_ge(out_done[ko], slot_count(t0, k, 9))
                    nc.vector.tensor_scalar(out_sb[:, ko, HALF:L], o_ps[:, h1, HALF:L], gain[:, h1:h1 + 1],
                                            shift[:, h1:h1 + 1], ALU.mult, ALU.add).then_inc(normed_dve, 1)

            step(0, 0)
            step(0, 1)
            dve.wait_ge(w_loaded, 16)
            nc.vector.tensor_scalar(wqT[:, :], w_in[:, 0, :], -SCALE, None, ALU.mult).then_inc(const_dve, 1)
            dve.wait_ge(c_loaded, 16 * N_CONST)
            nc.vector.tensor_scalar(bqB[:, :], rows[:, 0, :], -SCALE, None, ALU.mult).then_inc(const_dve, 1)
            nc.vector.tensor_scalar(bq_col[:, :], bq_raw, -SCALE * L, None, ALU.mult).then_inc(const_dve, 1)
            nc.vector.tensor_copy(ident[:, P:P + 1], bo).then_inc(const_dve, 1)
            dve.wait_ge(const_dve, 8)
            nc.vector.scalar_tensor_tensor(out=k0[:, :], in0=bkB, scalar=bq_col[:, :],
                                           in1=mask[:, :, :].rearrange("p h d -> p (h d)"),
                                           op0=ALU.mult, op1=ALU.add).then_inc(const_dve, 1)
            pipeline(dve, step, begin=2)

        @block.tensor
        def _(pe):
            def product(dst, lhsT, rhs, start=True, stop=True, **more):
                return nc.tensor.matmul(dst, lhsT, rhs, start=start, stop=stop, **more)

            def keep_busy(count):
                for _ in range(count):
                    product(o_ps[:, 1, 0:P], onesn[:, :], onesn[:, :])

            pe.wait_ge(const_dve, 1)
            keep_busy(WARM_UP)
            pe.wait_ge(const_dve, 4)

            def step(t0, k):
                t = t0 + k
                h = k % 2
                h1 = 1 - h

                def products_of_x(half):
                    cols_of = slice(half * HALF, (half + 1) * HALF)
                    product(o_ps[:, h, cols_of], m_sb[:, h, 0:E], x_sb[:, k, cols_of]).then_inc(o_ready, 1)

                def variance():
                    pe.wait_ge(vrow_ready, t - 4)
                    product(var_ps, onesn[:, :], vrow[:, h1:h1 + 1]).then_inc(var_ready, 1)

                def query_product():
                    pe.wait_ge(g_copied, t - 1)
                    if exists(t, 3):
                        pe.wait_ge(smin_ready, t - 2)
                    product(p_ps, g_sb[:, :], wqT[:, :]).then_inc(p_ready, 1)

                def softmax_product():
                    pe.wait_ge(a_ready, t - 2)
                    if exists(t, 4):
                        pe.wait_ge(m_copied, t - 3)
                    product(r_ps, a_sb[:, :], woT).then_inc(r_ready, 1)

                def mean():
                    pe.wait_ge(mrow_ready, t - 3)
                    if exists(t, 5):
                        pe.wait_ge(veps_ready, t - 4)
                    product(mu_ps, onesn[:, :], mrow[:, h:h + 1]).then_inc(mu_ready, 1)

                if has(t, 5) and late(t):
                    variance()
                if has(t, 4):
                    pe.wait_ge(m_copied, t - 3)
                    pe.wait_ge(x_in[k], slot_count(t0, k, 4))
                    if exists(t, 6):
                        pe.wait_ge(normed, t - 5)
                    products_of_x(0)
                if has(t, 5) and not late(t):
                    variance()
                if has(t, 2):
                    pe.wait_ge(b2_copied, t - 1)
                    product(g_ps[:, 0:C], b2_sb[:, :], ident_r[:, :], start=False, skip_group_check=True)
                    if first_steps(t, 2):
                        keep_busy(FILL[1])
                    pe.wait_ge(lsum_ready, t - 1)
                    product(g_ps[:, 2 * C:HL], lsum[:, h, :], ones_r[:, :], start=False,
                            skip_group_check=True).then_inc(g_ready, 1)
                if first_steps(t, 2):
                    keep_busy(FILL[2])
                if first_steps(t, 3):
                    keep_busy(FILL[3])
                if has(t, 3) and late(t):
                    softmax_product()
                if has(t, 4):
                    products_of_x(1)
                if has(t, 2):
                    query_product()
                if has(t, 3) and not late(t):
                    softmax_product()
                if has(t, 1):
                    kg = (k - 1) % UNROLL
                    pe.wait_ge(l_ready, t * 2)
                    if exists(t, 2):
                        pe.wait_ge(s_copied, t - 1)
                    for c in range(CH):
                        mm = product(g_ps[:, 0:HL], hl_sb[:, kg, c, 0:C], hl_sb[:, kg, c, :],
                                     start=(c == 0), stop=(c == CH - 1))
                    mm.then_inc(hl_ready, 1)
                if first_steps(t, 1):
                    keep_busy(FILL[0])
                if has(t, 3):
                    pe.wait_ge(r_copied, t - 2)
                    product(m_ps[:, 0:E], wv, r_sb[:, :])
                    product(m_ps[:, E:E + 1], r_sb[:, :], bv).then_inc(m_ready, 1)
                if has(t, 4):
                    mean()
                if has(t, 2):
                    pe.wait_ge(p_copied, t - 1)
                    pe.wait_ge(sbk_ready, t - 1)
                    product(sc_ps, p_sb[:, :], wkT, stop=False)
                    product(sc_ps, wqT[:, :], sbk_sb[:, :], start=False).then_inc(sc_ready, 1)
                if first_steps(t, 2):
                    keep_busy(FILL[4])
                if first_steps(t, 3):
                    keep_busy(FILL[5])

            step(0, 0)
            step(0, 1)
            pe.wait_ge(w_loaded, 16)
            pe.wait_ge(c_loaded, 16 * N_CONST)
            pe.wait_ge(const_dve, 5)
            pipeline(pe, step, begin=2)


_INS = ['x', 'ctx', 'weights', 'biases', 'columns']
_OUTS = [((32, 128, 1024), 'float32')]


def kernel(x, ctx_4096, L0_xattn_Wq, L0_xattn_bq, L0_xattn_Wk, L0_xattn_bk, L0_xattn_Wv, L0_xattn_bv,
           L0_xattn_Wo, L0_xattn_bo, L0_xattn_gn_w, L0_xattn_gn_b):
    import numpy as _np
    import concourse.bacc as _bacc
    from concourse import mybir as _mybir
    from concourse.bass_utils import run_bass_kernel_spmd as _run

    Wq, Wk, Wv, Wo = (_np.asarray(w) for w in (L0_xattn_Wq, L0_xattn_Wk, L0_xattn_Wv, L0_xattn_Wo))
    laid_out = {
        "x": _np.asarray(x),
        "ctx": _np.swapaxes(_np.asarray(ctx_4096), 1, 2),
        "weights": _np.concatenate([Wq.T, Wk.T, Wo.T, Wv], axis=1),
        "biases": _np.stack([_np.asarray(v) for v in (L0_xattn_bq, L0_xattn_bk)]),
        "columns": _np.stack([_np.asarray(v) for v in (L0_xattn_bq, L0_xattn_bk, L0_xattn_bv, L0_xattn_bo,
                                                       L0_xattn_gn_w, L0_xattn_gn_b)], axis=1),
    }
    nc = _bacc.Bacc("TRN2", target_bir_lowering=False, num_devices=1)
    arrays, args = {}, []
    for name in _INS:
        a = _np.ascontiguousarray(laid_out[name])
        arrays[f"in_{name}_dram"] = a
        args.append(nc.dram_tensor(f"in_{name}_dram", a.shape, _mybir.dt.from_np(a.dtype), kind="ExternalInput").ap())
    for i, (shape, dtype) in enumerate(_OUTS):
        dt = _mybir.dt.from_np(_np.dtype(dtype))
        args.append(nc.dram_tensor(f"out_{i}_dram", shape, dt, kind="ExternalOutput").ap())
    xattn_groupnorm_kernel(nc, *args)
    r = _run(nc, [arrays], core_ids=[0])
    got = tuple(r.results[0][f"out_{i}_dram"] for i in range(len(_OUTS)))
    return got[0]
```

```python
from contextlib import ExitStack

import concourse.bass as bass
from concourse import mybir

ALU = mybir.AluOpType
ACT = mybir.ActivationFunctionType
F32 = mybir.dt.float32
F32R = mybir.dt.float32r

HEADS = 8
EPS = 1e-5
OFF_HEAD = 1e30
UNROLL = 4
N_CONST = 2
LAGS = 5
GRAM_BEFORE_M = 6
WARM_UP = 12
FILL = 2


def xattn_groupnorm_kernel(nc, x, yT, weights, biases, columns, out):
    B, E, L = x.shape
    C = yT.shape[2]
    P = 128
    assert E == P and C == P and L % (4 * P) == 0 and B % UNROLL == 0
    DH = E // HEADS
    CH = L // P
    HALF = L // 2
    HCH = CH // 2
    HL = 2 * C + 2
    SCALE = float(E) ** -0.5

    with ExitStack() as ctx:
        def sb(name, shape, dt=F32):
            return ctx.enter_context(nc.sbuf_tensor(name, shape, dt))

        def ps(name, shape, dt=F32):
            return ctx.enter_context(nc.psum_tensor(name, shape, dt))

        def sem(name):
            return ctx.enter_context(nc.semaphore(name))

        y_sb = sb("y_sb", [P, UNROLL, CH, C])
        x_sb = sb("x_sb", [P, UNROLL, L])
        out_sb = sb("out_sb", [P, UNROLL, L])
        hl_sb = sb("hl_sb", [P, UNROLL, CH, HL], F32R)
        lsum4 = sb("lsum4", [P, CH // 2, C])
        lsum2 = sb("lsum2", [P, CH // 4, C])
        lsum = sb("lsum", [P, 2, C], F32R)
        b2_sb = sb("b2_sb", [P, C], F32R)
        g_sb = sb("g_sb", [P, C])
        s_sb = sb("s_sb", [P, 1])
        p_sb = sb("p_sb", [P, E])
        sbk_sb = sb("sbk_sb", [P, E])
        sc_sb = sb("sc_sb", [P, E])
        a_sb = sb("a_sb", [P, E])
        r_sb = sb("r_sb", [P, E])
        m_sb = sb("m_sb", [P, 2, E + 1])
        smin = sb("smin", [P, 2])
        zsum = sb("zsum", [P, 2])
        zinv = sb("zinv", [P, 2])
        bn = sb("bn", [P, 2, 2, 6])
        mv = sb("mv", [P, 2, 2])
        mrow = sb("mrow", [P, 2])
        dev = sb("dev", [P, 2])
        vrow = sb("vrow", [P, 2])
        veps = sb("veps", [P, 2])
        rstd = sb("rstd", [P, 2])
        nshift = sb("nshift", [P, 2])
        gain = sb("gain", [P, 2])
        shift = sb("shift", [P, 2])
        w_in = sb("w_in", [P, 4, P])
        wkT, woT, wv = w_in[:, 1, :], w_in[:, 2, :], w_in[:, 3, :]
        wqT = sb("wqT", [P, P])
        ident = sb("ident", [P, P + 1])
        ident_r = sb("ident_r", [P, P], F32R)
        onesn = sb("onesn", [P, P])
        ones_r = sb("ones_r", [P, 2], F32R)
        mask = sb("mask", [P, HEADS, DH])
        rows = sb("rows", [P, 2, E])
        bqB = sb("bqB", [P, E])
        bq_col = sb("bq_col", [P, 1])
        k0 = sb("k0", [P, E])
        cols = sb("cols", [P, 6])
        bkB = rows[:, 1, :]
        bq_raw, bv, bo, gn_w, gn_b = cols[:, 0:1], cols[:, 2:3], cols[:, 3:4], cols[:, 4:5], cols[:, 5:6]
        nhalf = sb("nhalf", [P, 1])
        warm = sb("warm", [P, 1])

        g_ps = ps("g_ps", [P, 512])
        ps_ps = ps("ps_ps", [P, 4, P])
        rm_ps = ps("rm_ps", [P, 512])
        st_ps = ps("st_ps", [P, 512])
        o_ps = ps("o_ps", [P, 2, L])
        p_ps, sc_ps, r_ps, m_ps = ps_ps[:, 0, :], ps_ps[:, 1, :], rm_ps[:, 0:P], rm_ps[:, 256:256 + E + 1]
        mu_ps, var_ps, s_ps = st_ps[:, 0:1], st_ps[:, 8:9], g_ps[:, 2 * C:2 * C + 1]

        y_in = [sem(f"y_in{k}") for k in range(UNROLL)]
        x_in = [sem(f"x_in{k}") for k in range(UNROLL)]
        out_done = [sem(f"out_done{k}") for k in range(UNROLL)]
        w_loaded = sem("w_loaded")
        c_loaded = sem("c_loaded")
        const_pool = sem("const_pool")
        const_dve = sem("const_dve")
        h_ready = sem("h_ready")
        l_ready = sem("l_ready")
        lsum4_ready = sem("lsum4_ready")
        lsum2_ready = sem("lsum2_ready")
        lsum_ready = sem("lsum_ready")
        hl_ready = sem("hl_ready")
        b2_copied = sem("b2_copied")
        g_ready = sem("g_ready")
        g_copied = sem("g_copied")
        s_copied = sem("s_copied")
        p_ready = sem("p_ready")
        p_copied = sem("p_copied")
        sbk_ready = sem("sbk_ready")
        sc_ready = sem("sc_ready")
        smin_ready = sem("smin_ready")
        exp_done = sem("exp_done")
        zinv_ready = sem("zinv_ready")
        a_ready = sem("a_ready")
        r_ready = sem("r_ready")
        r_copied = sem("r_copied")
        m_ready = sem("m_ready")
        m_copied = sem("m_copied")
        o_ready = sem("o_ready")
        bn_done = sem("bn_done")
        mv_ready = sem("mv_ready")
        mrow_ready = sem("mrow_ready")
        mu_ready = sem("mu_ready")
        dev_ready = sem("dev_ready")
        vrow_ready = sem("vrow_ready")
        var_ready = sem("var_ready")
        veps_ready = sem("veps_ready")
        rstd_ready = sem("rstd_ready")
        nshift_ready = sem("nshift_ready")
        gain_ready = sem("gain_ready")
        affine_ready = sem("affine_ready")
        normed = sem("normed")
        normed_dve = sem("normed_dve")

        def has(t, lag):
            return not isinstance(t, int) or 0 <= t - lag < B

        def exists(t, lag):
            return not isinstance(t, int) or t - lag >= 0

        RUSH = B + 2
        LAST = B + LAGS - 1

        def is_step(t, which):
            return isinstance(t, int) and t == which

        def slot_count(t0, k, lag):
            return t0 * (16 // UNROLL) + 16 * ((k - lag) // UNROLL + 1)

        def pipeline(eng, step, begin=0, first=2 * UNROLL, end=B):
            for t in range(begin, first):
                step(t - t % UNROLL, t % UNROLL)
            with eng.Fori(first, end - UNROLL + 1, UNROLL) as t0:
                for k in range(UNROLL):
                    step(t0, k)
            for t in range(end, B + LAGS):
                step(t - t % UNROLL, t % UNROLL)

        def batch(dram, b):
            return dram[bass.ds(b, 1)].rearrange("a p l -> p (a l)")

        def batch_y(b):
            return yT[bass.ds(b, 1)].rearrange("a (p j) c -> p (a j c)", p=P)

        def y_slot(k):
            return y_sb[:, k, :, :].rearrange("p j c -> p (j c)")

        block = ctx.enter_context(nc.Block())

        @block.sync
        def _(sp):
            for k in range(UNROLL):
                sp.dma_start(y_slot(k), batch_y(k)).then_inc(y_in[k], 16)

            def step(t0, k):
                t = t0 + k
                if has(t + UNROLL - 1, 0) and exists(t, 1):
                    ky = (k - 1) % UNROLL
                    sp.wait_ge(l_ready, t * 2)
                    sp.dma_start(y_slot(ky), batch_y(t + UNROLL - 1)).then_inc(y_in[ky], 16)
                if has(t, 0):
                    if exists(t, 4):
                        sp.wait_ge(o_ready, (t - (UNROLL - 1)) * 2)
                    sp.dma_start(x_sb[:, k, :], batch(x, t)).then_inc(x_in[k], 16)
                if is_step(t, LAST):
                    ko = (k - 5) % UNROLL
                    for half, done in ((0, normed), (1, normed_dve)):
                        part = slice(half * HALF, (half + 1) * HALF)
                        sp.wait_ge(done, B if half == 0 else 1)
                        sp.dma_start(batch(out, B - 1)[:, part], out_sb[:, ko, part]).then_inc(out_done[ko], 16)
                elif has(t, 5):
                    ko = (k - 5) % UNROLL
                    sp.wait_ge(normed, t - 4)
                    sp.dma_start(batch(out, t - 5), out_sb[:, ko, :]).then_inc(out_done[ko], 16)

            pipeline(sp, step, end=B - UNROLL)
            for k in range(UNROLL):
                sp.wait_ge(out_done[k], 16 * (B // UNROLL + (k == (B - 1) % UNROLL)))

        @block.gpsimd
        def _(pool):
            nc.gpsimd.memset(nhalf[:, :], -0.5).then_inc(const_pool, 1)
            nc.gpsimd.memset(ident[:, 0:P], 0.0).then_inc(const_pool, 1)
            nc.gpsimd.memset(mask[:, :, :], 0.0).then_inc(const_pool, 1)
            pool.wait_ge(const_pool, 3)
            nc.gpsimd.affine_select(out=ident[:, 0:P], in_=ident[:, 0:P], compare_op=ALU.not_equal, fill=1.0,
                                    base=0, pattern=[[-1, P]], channel_multiplier=1).then_inc(const_pool, 1)
            nc.gpsimd.affine_select(out=mask[:, :, :], in_=mask[:, :, :], compare_op=ALU.is_ge, fill=OFF_HEAD,
                                    base=0, pattern=[[-DH, HEADS], [0, DH]], channel_multiplier=1).then_inc(const_pool, 1)
            pool.wait_ge(const_pool, 5)
            nc.gpsimd.affine_select(out=mask[:, :, :], in_=mask[:, :, :], compare_op=ALU.is_ge, fill=OFF_HEAD,
                                    base=DH - 1, pattern=[[DH, HEADS], [0, DH]], channel_multiplier=-1).then_inc(const_pool, 1)

            def step(t0, k):
                t = t0 + k
                h = k % 2
                h1 = 1 - h
                if is_step(t, 5):
                    pool.wait_ge(c_loaded, 16 * N_CONST)
                if has(t, 5):
                    pool.wait_ge(dev_ready, t - 4)
                    nc.gpsimd.tensor_tensor(nshift[:, h1:h1 + 1], dev[:, h1:h1 + 1], mv[:, h1, 0:1],
                                            ALU.subtract).then_inc(nshift_ready, 1)
                    pool.wait_ge(veps_ready, t - 4)
                    nc.gpsimd.tensor_tensor(rstd[:, h1:h1 + 1], veps[:, h1:h1 + 1], nhalf[:, :], ALU.pow).then_inc(rstd_ready, 1)
                    pool.wait_ge(rstd_ready, t - 4)
                    nc.gpsimd.tensor_tensor(gain[:, h1:h1 + 1], rstd[:, h1:h1 + 1], gn_w, ALU.mult).then_inc(gain_ready, 1)
                    pool.wait_ge(c_loaded, 16 * N_CONST)
                    pool.wait_ge(nshift_ready, t - 4)
                    pool.wait_ge(gain_ready, t - 4)
                    nc.gpsimd.tensor_scalar(shift[:, h1:h1 + 1], nshift[:, h1:h1 + 1], gain[:, h1:h1 + 1], gn_b,
                                            ALU.mult, ALU.add).then_inc(affine_ready, 1)
                if has(t, 1):
                    low = hl_sb[:, (k - 1) % UNROLL, :, C:2 * C].bitcast(F32)
                    pool.wait_ge(l_ready, t * 2)
                    if exists(t, 2):
                        pool.wait_ge(lsum2_ready, t - 1)
                    nc.gpsimd.tensor_tensor(lsum4[:, :, :], low[:, 0:HCH, :], low[:, HCH:CH, :],
                                            ALU.add).then_inc(lsum4_ready, 1)
                    pool.wait_ge(lsum4_ready, t)
                    if exists(t, 2):
                        pool.wait_ge(lsum_ready, t - 1)
                    nc.gpsimd.tensor_tensor(lsum2[:, :, :], lsum4[:, 0:HCH // 2, :], lsum4[:, HCH // 2:HCH, :],
                                            ALU.add).then_inc(lsum2_ready, 1)
                    pool.wait_ge(lsum2_ready, t)
                    if exists(t, 3):
                        pool.wait_ge(g_ready, t - 2)
                    nc.gpsimd.tensor_tensor(lsum[:, h1, :], lsum2[:, 0, :], lsum2[:, 1, :], ALU.add).then_inc(lsum_ready, 1)

            pipeline(pool, step)

        @block.scalar
        def _(act):
            act.wait_ge(const_pool, 1)
            nc.scalar.activation(warm[:, :], nhalf[:, :], ACT.Exp)
            act.dma_start(cols[:, :], columns).then_inc(c_loaded, 16)
            act.dma_start(rows[:, :, :].rearrange("p v e -> p (v e)"),
                          biases.rearrange("(a v) e -> a (v e)", a=1).broadcast_to([P, 2 * E])).then_inc(c_loaded, 16)
            act.dma_start(w_in[:, :, :].rearrange("p w c -> p (w c)"), weights).then_inc(w_loaded, 16)

            def step(t0, k):
                t = t0 + k
                h = k % 2
                h1 = 1 - h
                if has(t, 3):
                    act.wait_ge(smin_ready, t - 2)
                    nc.scalar.activation(a_sb[:, :], sc_sb[:, :], ACT.Exp, bias=smin[:, h1:h1 + 1], scale=-1.0,
                                         accum_out=zsum[:, h1:h1 + 1]).then_inc(exp_done, 1)

                def round_half(half):
                    chunks = slice(half * HCH, (half + 1) * HCH)
                    nc.scalar.copy(hl_sb[:, k, chunks, 0:C], y_sb[:, k, chunks, :]).then_inc(h_ready, 1)

                if has(t, 0):
                    act.wait_ge(y_in[k], slot_count(t0, k, 0))
                    if exists(t, 4):
                        act.wait_ge(g_ready, t - 3)
                    round_half(0)
                if has(t, 3):
                    act.wait_ge(zinv_ready, t - 2)
                    nc.scalar.mul(a_sb[:, :], a_sb[:, :], zinv[:, h1:h1 + 1]).then_inc(a_ready, 1)
                if has(t, 2):
                    if is_step(t, 2):
                        act.wait_ge(c_loaded, 16 * N_CONST)
                    act.wait_ge(s_copied, t - 1)
                    nc.scalar.mul(sbk_sb[:, :], bkB, s_sb[:, :]).then_inc(sbk_ready, 1)
                if has(t, 3):
                    act.wait_ge(r_ready, t - 2)
                    nc.scalar.copy(r_sb[:, :], r_ps).then_inc(r_copied, 1)
                if has(t, 5):
                    ko = (k - 5) % UNROLL
                    act.wait_ge(affine_ready, t - 4)
                    if exists(t, 9):
                        act.wait_ge(out_done[ko], slot_count(t0, k, 9))
                    part = slice(0, HALF if is_step(t, LAST) else L)
                    nc.scalar.activation(out_sb[:, ko, part], o_ps[:, h1, part], ACT.Identity,
                                         bias=shift[:, h1:h1 + 1], scale=gain[:, h1:h1 + 1]).then_inc(normed, 1)
                ahead = is_step(t, 0) or is_step(t, 1)
                if ahead:
                    round_half(1)
                if has(t, 1):
                    act.wait_ge(hl_ready, t)
                    nc.scalar.copy(b2_sb[:, :], g_ps[:, C:2 * C]).then_inc(b2_copied, 1)
                if has(t, 0) and not ahead:
                    round_half(1)

            pipeline(act, step, first=3 * UNROLL)

        @block.vector
        def _(dve):
            nc.vector.memset(onesn[:, :], 1.0 / E).then_inc(const_dve, 1)
            nc.vector.memset(ones_r[:, :].bitcast(F32), 1.0).then_inc(const_dve, 1)
            nc.vector.memset(hl_sb[:, :, :, 2 * C:HL].bitcast(F32), 1.0).then_inc(const_dve, 1)
            dve.wait_ge(const_pool, 6)
            nc.vector.tensor_copy(ident_r[:, :], ident[:, 0:P]).then_inc(const_dve, 1)

            def value(v):
                return v if isinstance(v, int) else dve.to_reg(v)

            def step(t0, k):
                t = t0 + k
                h = k % 2
                h1 = 1 - h

                def folded_matrix():
                    dve.wait_ge(m_ready, t - 2)
                    nc.vector.tensor_tensor(m_sb[:, h1, :], m_ps, ident[:, :], ALU.add).then_inc(m_copied, 1)

                if has(t, 5):
                    dve.wait_ge(mu_ready, t - 4)
                    nc.vector.tensor_tensor(dev[:, h1:h1 + 1], mrow[:, h1:h1 + 1], mu_ps, ALU.subtract).then_inc(dev_ready, 1)
                    dve.wait_ge(dev_ready, t - 4)
                    nc.vector.scalar_tensor_tensor(out=vrow[:, h1:h1 + 1], in0=dev[:, h1:h1 + 1], scalar=dev[:, h1:h1 + 1],
                                                   in1=mv[:, h1, 1:2], op0=ALU.mult, op1=ALU.add).then_inc(vrow_ready, 1)
                if has(t, 3):
                    done = value(t - 2)
                    dve.wait_ge(const_dve, 9)
                    dve.wait_ge(sc_ready, done)
                    nc.vector.tensor_tensor_reduce(out=sc_sb[:, :], in0=sc_ps, in1=k0[:, :], scale=1.0,
                                                   scalar=3e38, op0=ALU.add, op1=ALU.min,
                                                   accum_out=smin[:, h1:h1 + 1]).then_inc(smin_ready, 1)

                def rest_half(b, half):
                    ky = (k + b) % UNROLL
                    chunks = slice(half * HCH, (half + 1) * HCH)
                    dve.wait_ge(h_ready, (t + b) * 2 + 1 + half)
                    nc.vector.tensor_tensor(hl_sb[:, ky, chunks, C:2 * C], y_sb[:, ky, chunks, :],
                                            hl_sb[:, ky, chunks, 0:C].bitcast(F32), ALU.subtract).then_inc(l_ready, 1)

                if has(t, 1):
                    rest_half(-1, 1)
                if is_step(t, 2):
                    dve.wait_ge(w_loaded, 16)
                    nc.vector.tensor_scalar(wqT[:, :], w_in[:, 0, :], -SCALE, None, ALU.mult).then_inc(const_dve, 1)
                def inverse_sums():
                    dve.wait_ge(exp_done, t - 2)
                    nc.vector.reciprocal(zinv[:, h1:h1 + 1], zsum[:, h1:h1 + 1]).then_inc(zinv_ready, 1)

                def variance():
                    dve.wait_ge(var_ready, t - 4)
                    nc.vector.tensor_scalar(veps[:, h1:h1 + 1], var_ps, EPS, None, ALU.add).then_inc(veps_ready, 1)

                def gram():
                    dve.wait_ge(g_ready, t - 1)
                    nc.vector.tensor_tensor(g_sb[:, :], g_ps[:, 0:C], b2_sb[:, :].bitcast(F32), ALU.add).then_inc(g_copied, 1)
                    nc.vector.tensor_copy(s_sb[:, :], s_ps).then_inc(s_copied, 1)

                def statistics():
                    dve.wait_ge(o_ready, (t - 4) * 2 + 1)
                    nc.vector.bn_stats(bn[:, h, 0, :], o_ps[:, h, 0:HALF])
                    if is_step(t, RUSH):
                        folded_matrix()
                    dve.wait_ge(o_ready, (t - 3) * 2)
                    nc.vector.bn_stats(bn[:, h, 1, :], o_ps[:, h, HALF:L]).then_inc(bn_done, 1)

                def query_product():
                    dve.wait_ge(s_copied, t - 1)
                    dve.wait_ge(p_ready, t - 1)
                    nc.vector.scalar_tensor_tensor(out=p_sb[:, :], in0=bqB[:, :], scalar=s_sb[:, :],
                                                   in1=p_ps, op0=ALU.mult, op1=ALU.add).then_inc(p_copied, 1)

                if has(t, 5) and is_step(t, RUSH):
                    variance()
                if has(t, 3):
                    inverse_sums()
                if has(t, 5) and not is_step(t, RUSH) and not is_step(t, RUSH + 1):
                    variance()
                if has(t, 2):
                    gram()
                if has(t, 4):
                    statistics()
                if is_step(t, RUSH + 1):
                    variance()
                if has(t, 2):
                    query_product()
                if has(t, 4):
                    done = value(t - 3)
                    dve.wait_ge(c_loaded, 16 * N_CONST)
                    dve.wait_ge(bn_done, done)
                    nc.vector.bn_aggr(mv[:, h, :], bn[:, h, :, :].rearrange("p a b -> p (a b)")).then_inc(mv_ready, 1)
                    dve.wait_ge(mv_ready, t - 3)
                    nc.vector.tensor_tensor(mrow[:, h:h + 1], m_sb[:, h, E:E + 1], mv[:, h, 0:1],
                                            ALU.add).then_inc(mrow_ready, 1)
                if has(t, 3) and not is_step(t, RUSH):
                    folded_matrix()
                if has(t, 0):
                    rest_half(0, 0)
                if is_step(t, LAST):
                    ko = (k - 5) % UNROLL
                    dve.wait_ge(affine_ready, B)
                    dve.wait_ge(out_done[ko], slot_count(t0, k, 9))
                    nc.vector.tensor_scalar(out_sb[:, ko, HALF:L], o_ps[:, h1, HALF:L], gain[:, h1:h1 + 1],
                                            shift[:, h1:h1 + 1], ALU.mult, ALU.add).then_inc(normed_dve, 1)

            step(0, 0)
            step(0, 1)
            dve.wait_ge(c_loaded, 16 * N_CONST)
            nc.vector.tensor_scalar(bqB[:, :], rows[:, 0, :], -SCALE, None, ALU.mult).then_inc(const_dve, 1)
            nc.vector.tensor_scalar(bq_col[:, :], bq_raw, -SCALE * L, None, ALU.mult).then_inc(const_dve, 1)
            nc.vector.tensor_copy(ident[:, P:P + 1], bo).then_inc(const_dve, 1)
            dve.wait_ge(const_dve, 7)
            nc.vector.scalar_tensor_tensor(out=k0[:, :], in0=bkB, scalar=bq_col[:, :],
                                           in1=mask[:, :, :].rearrange("p h d -> p (h d)"),
                                           op0=ALU.mult, op1=ALU.add).then_inc(const_dve, 1)
            pipeline(dve, step, begin=2)

        @block.tensor
        def _(pe):
            def product(dst, lhsT, rhs, start=True, stop=True, **more):
                return nc.tensor.matmul(dst, lhsT, rhs, start=start, stop=stop, **more)

            def keep_busy(count):
                for _ in range(count):
                    product(o_ps[:, 1, 0:P], onesn[:, :], onesn[:, :])

            pe.wait_ge(const_dve, 1)
            keep_busy(WARM_UP)
            pe.wait_ge(const_dve, 4)

            def step(t0, k):
                t = t0 + k
                h = k % 2
                h1 = 1 - h

                def products_of_x(half):
                    cols_of = slice(half * HALF, (half + 1) * HALF)
                    product(o_ps[:, h, cols_of], m_sb[:, h, 0:E], x_sb[:, k, cols_of]).then_inc(o_ready, 1)

                def variance():
                    pe.wait_ge(vrow_ready, t - 4)
                    product(var_ps, onesn[:, :], vrow[:, h1:h1 + 1]).then_inc(var_ready, 1)

                def query_product():
                    if is_step(t, 2):
                        pe.wait_ge(w_loaded, 16)
                        pe.wait_ge(c_loaded, 16 * N_CONST)
                        pe.wait_ge(const_dve, 9)
                    pe.wait_ge(g_copied, t - 1)
                    if exists(t, 3):
                        pe.wait_ge(smin_ready, t - 2)
                    product(p_ps, g_sb[:, :], wqT[:, :]).then_inc(p_ready, 1)

                def softmax_product():
                    pe.wait_ge(a_ready, t - 2)
                    if exists(t, 4):
                        pe.wait_ge(m_copied, t - 3)
                    product(r_ps, a_sb[:, :], woT).then_inc(r_ready, 1)

                def mean(b):
                    pe.wait_ge(mrow_ready, t + b + 1)
                    if exists(t, 1 - b):
                        pe.wait_ge(veps_ready, t + b)
                    row = (h + b) % 2
                    product(mu_ps, onesn[:, :], mrow[:, row:row + 1]).then_inc(mu_ready, 1)

                if has(t, 5) and is_step(t, RUSH):
                    variance()
                if has(t, 4):
                    pe.wait_ge(m_copied, t - 3)
                    pe.wait_ge(x_in[k], slot_count(t0, k, 4))
                    if exists(t, 6):
                        pe.wait_ge(normed, t - 5)
                    products_of_x(0)
                if is_step(t, RUSH + 1):
                    mean(-5)
                elif has(t, 5) and not is_step(t, RUSH):
                    variance()
                if has(t, 2):
                    pe.wait_ge(b2_copied, t - 1)
                    product(g_ps[:, 0:C], b2_sb[:, :], ident_r[:, :], start=False, skip_group_check=True)
                    if is_step(t, 2):
                        keep_busy(FILL)
                    pe.wait_ge(lsum_ready, t - 1)
                    product(g_ps[:, 2 * C:HL], lsum[:, h, :], ones_r[:, :], start=False,
                            skip_group_check=True).then_inc(g_ready, 1)
                if is_step(t, 2):
                    keep_busy(FILL)
                if has(t, 3) and is_step(t, RUSH):
                    softmax_product()
                if has(t, 4):
                    products_of_x(1)
                if is_step(t, RUSH + 1):
                    variance()
                if has(t, 2):
                    query_product()
                if has(t, 3) and not is_step(t, RUSH):
                    softmax_product()

                def gram_products(chunks):
                    kg = (k - 1) % UNROLL
                    for c in chunks:
                        mm = product(g_ps[:, 0:HL], hl_sb[:, kg, c, 0:C], hl_sb[:, kg, c, :],
                                     start=(c == 0), stop=(c == CH - 1))
                    return mm

                if has(t, 1):
                    pe.wait_ge(l_ready, t * 2)
                    if exists(t, 2):
                        pe.wait_ge(s_copied, t - 1)
                    gram_products(range(0, GRAM_BEFORE_M))
                if has(t, 3):
                    pe.wait_ge(r_copied, t - 2)
                    product(m_ps[:, 0:E], wv, r_sb[:, :])
                    product(m_ps[:, E:E + 1], r_sb[:, :], bv).then_inc(m_ready, 1)
                if has(t, 1):
                    gram_products(range(GRAM_BEFORE_M, CH)).then_inc(hl_ready, 1)
                if is_step(t, 1):
                    keep_busy(FILL)
                if has(t, 4) and not is_step(t, RUSH):
                    mean(-4)
                if has(t, 2):
                    pe.wait_ge(p_copied, t - 1)
                    pe.wait_ge(sbk_ready, t - 1)
                    product(sc_ps, p_sb[:, :], wkT, stop=False)
                    product(sc_ps, wqT[:, :], sbk_sb[:, :], start=False).then_inc(sc_ready, 1)

            pipeline(pe, step)


_INS = ['x', 'ctx', 'weights', 'biases', 'columns']
_OUTS = [((32, 128, 1024), 'float32')]


def kernel(x, ctx_4096, L0_xattn_Wq, L0_xattn_bq, L0_xattn_Wk, L0_xattn_bk, L0_xattn_Wv, L0_xattn_bv,
           L0_xattn_Wo, L0_xattn_bo, L0_xattn_gn_w, L0_xattn_gn_b):
    import numpy as _np
    import concourse.bacc as _bacc
    from concourse import mybir as _mybir
    from concourse.bass_utils import run_bass_kernel_spmd as _run

    Wq, Wk, Wv, Wo = (_np.asarray(w) for w in (L0_xattn_Wq, L0_xattn_Wk, L0_xattn_Wv, L0_xattn_Wo))
    laid_out = {
        "x": _np.asarray(x),
        "ctx": _np.swapaxes(_np.asarray(ctx_4096), 1, 2),
        "weights": _np.concatenate([Wq.T, Wk.T, Wo.T, Wv], axis=1),
        "biases": _np.stack([_np.asarray(v) for v in (L0_xattn_bq, L0_xattn_bk)]),
        "columns": _np.stack([_np.asarray(v) for v in (L0_xattn_bq, L0_xattn_bk, L0_xattn_bv, L0_xattn_bo,
                                                       L0_xattn_gn_w, L0_xattn_gn_b)], axis=1),
    }
    nc = _bacc.Bacc("TRN2", target_bir_lowering=False, num_devices=1)
    arrays, args = {}, []
    for name in _INS:
        a = _np.ascontiguousarray(laid_out[name])
        arrays[f"in_{name}_dram"] = a
        args.append(nc.dram_tensor(f"in_{name}_dram", a.shape, _mybir.dt.from_np(a.dtype), kind="ExternalInput").ap())
    for i, (shape, dtype) in enumerate(_OUTS):
        dt = _mybir.dt.from_np(_np.dtype(dtype))
        args.append(nc.dram_tensor(f"out_{i}_dram", shape, dt, kind="ExternalOutput").ap())
    xattn_groupnorm_kernel(nc, *args)
    r = _run(nc, [arrays], core_ids=[0])
    got = tuple(r.results[0][f"out_{i}_dram"] for i in range(len(_OUTS)))
    return got[0]
```
